# Optimizing a Trainium2 kernel written in Bass

```python
import numpy as np
import jax
import jax.numpy as jnp

def _softmax(x, axis=-1):
    return jax.nn.softmax(x, axis=axis)

def _gelu(x):
    return jax.nn.gelu(x, approximate=True)

def _silu(x):
    return jax.nn.silu(x)

def _sigmoid(x):
    return jax.nn.sigmoid(x)

def _layernorm(x, axis=-1, eps=1e-05):
    m = jnp.mean(x, axis=axis, keepdims=True)
    v = jnp.var(x, axis=axis, keepdims=True)
    return (x - m) / jnp.sqrt(v + eps)

def _scatter_add(tgt, idx, src, axis=0):
    return tgt.at[idx].add(src)

def _segment_sum(src, seg, n):
    return jax.ops.segment_sum(src, seg, n)
kernel_name = 'mk_dlrm_tower_d1_rec_r8_55998f'

def setup_inputs(seed: int=0):
    np.random.seed(seed)
    _w = jnp.asarray

    def _rec_inputs():
        import jax
        import jax.numpy as jnp
        _tk = jax.random.key(seed)
        ids = jnp.stack([jax.random.randint(jax.random.fold_in(_tk, 200 + f), (512,), 0, v, jnp.int32) for f, v in enumerate([125000, 1250, 1000, 12500, 1000, 12500, 1250, 1000, 1250, 1000, 1000, 12500, 1000, 1000, 12500, 1000, 1250, 12500, 1250, 12500, 1250, 1000, 1000, 1000, 1250, 1000])], axis=1)
        tbl_0 = 0.05 * jax.random.normal(jax.random.fold_in(_tk, 500 + 0), (125000, 128), jnp.float32)
        tbl_1 = 0.05 * jax.random.normal(jax.random.fold_in(_tk, 500 + 1), (1250, 128), jnp.float32)
        tbl_2 = 0.05 * jax.random.normal(jax.random.fold_in(_tk, 500 + 2), (1000, 128), jnp.float32)
        tbl_3 = 0.05 * jax.random.normal(jax.random.fold_in(_tk, 500 + 3), (12500, 128), jnp.float32)
        tbl_4 = 0.05 * jax.random.normal(jax.random.fold_in(_tk, 500 + 4), (1000, 128), jnp.float32)
        tbl_5 = 0.05 * jax.random.normal(jax.random.fold_in(_tk, 500 + 5), (12500, 128), jnp.float32)
        tbl_6 = 0.05 * jax.random.normal(jax.random.fold_in(_tk, 500 + 6), (1250, 128), jnp.float32)
        tbl_7 = 0.05 * jax.random.normal(jax.random.fold_in(_tk, 500 + 7), (1000, 128), jnp.float32)
        tbl_8 = 0.05 * jax.random.normal(jax.random.fold_in(_tk, 500 + 8), (1250, 128), jnp.float32)
        tbl_9 = 0.05 * jax.random.normal(jax.random.fold_in(_tk, 500 + 9), (1000, 128), jnp.float32)
        tbl_10 = 0.05 * jax.random.normal(jax.random.fold_in(_tk, 500 + 10), (1000, 128), jnp.float32)
        tbl_11 = 0.05 * jax.random.normal(jax.random.fold_in(_tk, 500 + 11), (12500, 128), jnp.float32)
        tbl_12 = 0.05 * jax.random.normal(jax.random.fold_in(_tk, 500 + 12), (1000, 128), jnp.float32)
        tbl_13 = 0.05 * jax.random.normal(jax.random.fold_in(_tk, 500 + 13), (1000, 128), jnp.float32)
        tbl_14 = 0.05 * jax.random.normal(jax.random.fold_in(_tk, 500 + 14), (12500, 128), jnp.float32)
        tbl_15 = 0.05 * jax.random.normal(jax.random.fold_in(_tk, 500 + 15), (1000, 128), jnp.float32)
        tbl_16 = 0.05 * jax.random.normal(jax.random.fold_in(_tk, 500 + 16), (1250, 128), jnp.float32)
        tbl_17 = 0.05 * jax.random.normal(jax.random.fold_in(_tk, 500 + 17), (12500, 128), jnp.float32)
        tbl_18 = 0.05 * jax.random.normal(jax.random.fold_in(_tk, 500 + 18), (1250, 128), jnp.float32)
        tbl_19 = 0.05 * jax.random.normal(jax.random.fold_in(_tk, 500 + 19), (12500, 128), jnp.float32)
        tbl_20 = 0.05 * jax.random.normal(jax.random.fold_in(_tk, 500 + 20), (1250, 128), jnp.float32)
        tbl_21 = 0.05 * jax.random.normal(jax.random.fold_in(_tk, 500 + 21), (1000, 128), jnp.float32)
        tbl_22 = 0.05 * jax.random.normal(jax.random.fold_in(_tk, 500 + 22), (1000, 128), jnp.float32)
        tbl_23 = 0.05 * jax.random.normal(jax.random.fold_in(_tk, 500 + 23), (1000, 128), jnp.float32)
        tbl_24 = 0.05 * jax.random.normal(jax.random.fold_in(_tk, 500 + 24), (1250, 128), jnp.float32)
        tbl_25 = 0.05 * jax.random.normal(jax.random.fold_in(_tk, 500 + 25), (1000, 128), jnp.float32)
        _rk = jax.random.fold_in(_tk, 7)
        r_dense_features = -0.000520686 + 1.00062 * jax.random.normal(jax.random.fold_in(_rk, 101), (512, 128), jnp.float32)
        W_top1 = 0.0405887 * jax.random.normal(jax.random.fold_in(_tk, 801), (607, 512), jnp.float32)
        W_top2 = 0.0441942 * jax.random.normal(jax.random.fold_in(_tk, 802), (512, 256), jnp.float32)
        W_top3 = 0.0625 * jax.random.normal(jax.random.fold_in(_tk, 803), (256, 1), jnp.float32)
        b_top1 = jnp.zeros((512,), jnp.float32)
        b_top2 = jnp.zeros((256,), jnp.float32)
        return (r_dense_features, ids, tbl_0, tbl_1, tbl_2, tbl_3, tbl_4, tbl_5, tbl_6, tbl_7, tbl_8, tbl_9, tbl_10, tbl_11, tbl_12, tbl_13, tbl_14, tbl_15, tbl_16, tbl_17, tbl_18, tbl_19, tbl_20, tbl_21, tbl_22, tbl_23, tbl_24, tbl_25, W_top1, b_top1, W_top2, b_top2, W_top3)
    r_dense_features, ids, tbl_0, tbl_1, tbl_2, tbl_3, tbl_4, tbl_5, tbl_6, tbl_7, tbl_8, tbl_9, tbl_10, tbl_11, tbl_12, tbl_13, tbl_14, tbl_15, tbl_16, tbl_17, tbl_18, tbl_19, tbl_20, tbl_21, tbl_22, tbl_23, tbl_24, tbl_25, W_top1, b_top1, W_top2, b_top2, W_top3 = _rec_inputs()

    def _L0_rec_setup():
        import jax, jax.numpy as jnp
        import numpy as np
        F = 26
        N = F + 1
        _TRIU_I, _TRIU_J = np.triu_indices(N, k=1)
        key = jax.random.key(seed)
        k1, k2 = jax.random.split(key)
        B, D = (2048, 128)
        dense_features = jax.random.normal(k1, (B, D), dtype=jnp.float32)
        sparse_features = jax.random.normal(k2, (B, F, D), dtype=jnp.float32)
        return {'dense_features': dense_features, 'sparse_features': sparse_features}
    _L0_rec_all = _L0_rec_setup()
    _L0_rec_in = {k: v for k, v in _L0_rec_all.items() if k in ()}
    del _L0_rec_all
    return {'r_dense_features': r_dense_features, 'ids': ids, 'tbl_0': tbl_0, 'tbl_1': tbl_1, 'tbl_2': tbl_2, 'tbl_3': tbl_3, 'tbl_4': tbl_4, 'tbl_5': tbl_5, 'tbl_6': tbl_6, 'tbl_7': tbl_7, 'tbl_8': tbl_8, 'tbl_9': tbl_9, 'tbl_10': tbl_10, 'tbl_11': tbl_11, 'tbl_12': tbl_12, 'tbl_13': tbl_13, 'tbl_14': tbl_14, 'tbl_15': tbl_15, 'tbl_16': tbl_16, 'tbl_17': tbl_17, 'tbl_18': tbl_18, 'tbl_19': tbl_19, 'tbl_20': tbl_20, 'tbl_21': tbl_21, 'tbl_22': tbl_22, 'tbl_23': tbl_23, 'tbl_24': tbl_24, 'tbl_25': tbl_25, 'W_top1': W_top1, 'b_top1': b_top1, 'W_top2': W_top2, 'b_top2': b_top2, 'W_top3': W_top3}

def reference(r_dense_features, ids, tbl_0, tbl_1, tbl_2, tbl_3, tbl_4, tbl_5, tbl_6, tbl_7, tbl_8, tbl_9, tbl_10, tbl_11, tbl_12, tbl_13, tbl_14, tbl_15, tbl_16, tbl_17, tbl_18, tbl_19, tbl_20, tbl_21, tbl_22, tbl_23, tbl_24, tbl_25, W_top1, b_top1, W_top2, b_top2, W_top3):
    import jax
    import jax.numpy as jnp

    def _L0_rec_ref(dense_features, sparse_features):
        import jax, jax.numpy as jnp
        import numpy as np
        F = 26
        N = F + 1
        _TRIU_I, _TRIU_J = np.triu_indices(N, k=1)
        combined = jnp.concatenate([dense_features[:, None, :], sparse_features], axis=1)
        interactions = jnp.einsum('bnd,bmd->bnm', combined, combined)
        interactions_flat = interactions[:, _TRIU_I, _TRIU_J]
        return jnp.concatenate([dense_features, interactions_flat], axis=1)
    e = jnp.stack([tbl_0[ids[:, 0]], tbl_1[ids[:, 1]], tbl_2[ids[:, 2]], tbl_3[ids[:, 3]], tbl_4[ids[:, 4]], tbl_5[ids[:, 5]], tbl_6[ids[:, 6]], tbl_7[ids[:, 7]], tbl_8[ids[:, 8]], tbl_9[ids[:, 9]], tbl_10[ids[:, 10]], tbl_11[ids[:, 11]], tbl_12[ids[:, 12]], tbl_13[ids[:, 13]], tbl_14[ids[:, 14]], tbl_15[ids[:, 15]], tbl_16[ids[:, 16]], tbl_17[ids[:, 17]], tbl_18[ids[:, 18]], tbl_19[ids[:, 19]], tbl_20[ids[:, 20]], tbl_21[ids[:, 21]], tbl_22[ids[:, 22]], tbl_23[ids[:, 23]], tbl_24[ids[:, 24]], tbl_25[ids[:, 25]]], axis=1)
    z = _L0_rec_ref(r_dense_features, e)
    z = z.reshape(z.shape[0], -1)
    h = jnp.concatenate([z, r_dense_features], axis=1)
    h = jnp.maximum(h @ W_top1 + b_top1, 0.0)
    h = jnp.maximum(h @ W_top2 + b_top2, 0.0)
    y = h @ W_top3
    return y

_drawn_inputs = setup_inputs


def setup_inputs(seed=0):
    import zlib

    import numpy as np

    out = dict(_drawn_inputs(seed))
    spreads = {'b_top1': (0.0, 0.1), 'b_top2': (0.0, 0.1)}
    factors = {}
    for name, (base, spread) in spreads.items():
        noise = np.random.default_rng([zlib.crc32(name.encode()), seed]).standard_normal(out[name].shape)
        drawn = base * np.exp(spread * noise) if base else spread * noise
        out[name] = jnp.asarray(drawn.astype(out[name].dtype))
    for name, factor in factors.items():
        out[name] = (out[name] * factor).astype(out[name].dtype)
    return out
```

```python
from contextlib import ExitStack

import concourse.bass as bass
import numpy as np
from concourse import mybir

F32 = mybir.dt.float32
F32R = mybir.dt.float32r
I32 = mybir.dt.int32
U32 = mybir.dt.uint32
ALU = mybir.AluOpType
ACT = mybir.ActivationFunctionType

P = 128
BATCH = 512
TILES = BATCH // P
DIM = 128
NUM_TABLES = 26
NODES = NUM_TABLES + 1
SLOTS = 32
QUAD = 32
QUADS = P // QUAD
TABLE_ROWS = [125000, 1250, 1000, 12500, 1000, 12500, 1250, 1000, 1250, 1000, 1000, 12500, 1000,
              1000, 12500, 1000, 1250, 12500, 1250, 12500, 1250, 1000, 1000, 1000, 1250, 1000]
PICK_PARTS = 125
PICK_ROWS = 8
NUM_PICKED = 7
PICKED = [f for f, rows in enumerate(TABLE_ROWS) if rows == PICK_PARTS * PICK_ROWS][:NUM_PICKED]
GATHERED = [f for f in range(NUM_TABLES) if f not in PICKED]
NODE_AT = [0] + [1 + f for f in PICKED + GATHERED]
FIRST_GATHERED = 1 + NUM_PICKED

GROUPS = [range(s, min(s + 4, len(GATHERED))) for s in range(0, len(GATHERED), 4)]
NG = len(GROUPS)
GATHER_RING = 3

LOW = 3
CHUNKS = (NODES - LOW) // QUADS
SPARE_PAIRS = [(0, 27, 0, 1), (1, 27, 0, 2), (1, 28, 1, 2)]
H1, H2 = 512, 256
K1, K2 = H1 // P, H2 // P


def pair_rows():
    places = [(QUAD * ((c - LOW) % QUADS) + i, (c - LOW) // QUADS, i, c)
              for c in range(LOW, NODES) for i in range(c)]
    places += [(QUAD * q + row, 0, i, c) for q, row, i, c in SPARE_PAIRS]
    out = []
    for part, chunk, i, c in places:
        a, b = sorted((NODE_AT[i], NODE_AT[c]))
        out.append((part, chunk, DIM + a * NODES - a * (a + 1) // 2 + (b - a - 1)))
    return out


def mover(tile, group):
    return "scalar" if tile == 0 or group % 2 == 0 else "vector"


def moved_count(engine, tile, group):
    return sum(mover(t, g) == engine for t in range(tile + 1) for g in range(NG)
               if (t, g) <= (tile, group))


def build(nc, dense, ids, ids_picked, tables, w1, w2, w3, b1, b2, out):
    with ExitStack() as ctx:
        def sb(name, shape, dt=F32):
            return ctx.enter_context(nc.sbuf_tensor(name, shape, dt))

        def psum(name, shape):
            return ctx.enter_context(nc.psum_tensor(name, shape, F32))

        def sem(name):
            return ctx.enter_context(nc.semaphore(name))

        ids_sb = sb("ids_sb", [P, TILES, NUM_TABLES], I32)
        ids_row = sb("ids_row", [PICK_PARTS, NUM_PICKED, BATCH], I32)
        dense_sb = sb("dense_sb", [P, TILES, DIM])
        w1_sb = sb("w1_sb", [P, CHUNKS + 2, H1])
        w2_sb = sb("w2_sb", [P, K1, H2])
        w3_sb = sb("w3_sb", [P, K2])
        b1_sb = sb("b1_sb", [P, K1])
        b2_sb = sb("b2_sb", [P, K2])
        identity = sb("identity", [P, P])
        row_number = sb("row_number", [P, PICK_ROWS])
        table_raw = sb("table_raw", [PICK_PARTS, 2, PICK_ROWS, DIM])
        table_hi = sb("table_hi", [PICK_PARTS, 2, PICK_ROWS, DIM], F32R)
        table_lo = sb("table_lo", [PICK_PARTS, 2, PICK_ROWS, DIM], F32R)
        onehot = sb("onehot", [PICK_PARTS, 2, PICK_ROWS, BATCH], F32R)
        rows = sb("rows", [P, GATHER_RING, len(GATHERED), DIM])
        dense_t = sb("dense_t", [DIM, BATCH])
        cols = sb("cols", [DIM, BATCH, SLOTS])
        z = sb("z", [P, 2, CHUNKS, P])
        h1 = sb("h1", [P, 2, K1, P])
        h2 = sb("h2", [P, 2, K2, P])
        y_sb = sb("y_sb", [1, BATCH])

        acc_ps = [psum("acc_ps0", [P, 512]), psum("acc_ps1", [P, 512])]
        turn_ps = [psum("turn_ps0", [P, 4, P]), psum("turn_ps1", [P, 4, P])]
        dots_ps = psum("dots_ps", [P, QUAD, SLOTS])
        h2_ps = [psum("h2_ps0", [P, 512]), psum("h2_ps1", [P, 512])]
        y_ps = h2_ps[1][0:1, P:2 * P]

        ids_in = sem("ids_in")
        ids_row_in = sem("ids_row_in")
        dense_in = sem("dense_in")
        w1_in = sem("w1_in")
        w2_in = sem("w2_in")
        small_in = sem("small_in")
        table_in = [sem("table_in0"), sem("table_in1")]
        rows_in = [[sem(f"rows_in{t}_{g}") for g in range(NG)] for t in range(TILES)]
        ones_ready = sem("ones_ready")
        identity_ready = sem("identity_ready")
        numbers_ready = sem("numbers_ready")
        cleared = sem("cleared")
        hi_ready = sem("hi_ready")
        lo_ready = sem("lo_ready")
        onehot_ready = sem("onehot_ready")
        picked_done = sem("picked_done")
        picked_moved = sem("picked_moved")
        dense_turned = sem("dense_turned")
        dense_t_ready = sem("dense_t_ready")
        dense_cols_ready = sem("dense_cols_ready")
        turned = sem("turned")
        turned_moved = {"scalar": sem("turned_moved_act"), "vector": sem("turned_moved_dve")}
        dots_done = sem("dots_done")
        spare_moved = {"scalar": sem("spare_moved_act"), "vector": sem("spare_moved_dve")}
        z_ready = {"scalar": sem("z_ready_act"), "vector": sem("z_ready_dve")}
        w1_folded = sem("w1_folded")
        layer1_done = sem("layer1_done")
        h1_ready = {"scalar": sem("h1_ready_act"), "vector": sem("h1_ready_dve")}
        layer2_done = sem("layer2_done")
        h2_ready = {"scalar": sem("h2_ready_act"), "vector": sem("h2_ready_dve")}
        layer3_done = sem("layer3_done")
        y_moved = sem("y_moved")
        out_done = sem("out_done")

        block = ctx.enter_context(nc.Block())

        @block.sync
        def _(sp):
            sp.dma_start(ids_sb[:], ids.rearrange("(t p) f -> p t f", p=P)).then_inc(ids_in, 16)

            def load_table(k):
                src = tables[PICKED[k]].rearrange("(p c) d -> p c d", c=PICK_ROWS)
                sp.dma_start(table_raw[:, k % 2], src).then_inc(table_in[k % 2], 16)

            load_table(0)
            sp.dma_start(dense_sb[:], dense.rearrange("(t p) d -> p t d", p=P)).then_inc(dense_in, 16)
            load_table(1)
            for k in range(2, NUM_PICKED):
                sp.wait_ge(lo_ready, k - 1)
                load_table(k)
            sp.wait_ge(y_moved, TILES)
            sp.dma_start(out.rearrange("(o b) c -> o (b c)", o=1), y_sb[:]).then_inc(out_done, 16)
            sp.wait_ge(out_done, 16)

        @block.gpsimd
        def _(pool):
            nc.gpsimd.iota(row_number[:], pattern=[[1, PICK_ROWS]], base=0, channel_multiplier=PICK_ROWS,
                           allow_small_or_imprecise_dtypes=True).then_inc(numbers_ready, 1)
            nc.gpsimd.memset(identity[:], 1.0).then_inc(ones_ready, 1)
            pool.wait_ge(ones_ready, 1)
            nc.gpsimd.affine_select(out=identity[:], in_=identity[:], compare_op=ALU.is_equal, fill=0.0,
                                    base=0, pattern=[[-1, P]],
                                    channel_multiplier=1).then_inc(identity_ready, 1)
            pool.wait_ge(ids_in, 16)
            for t in range(TILES):
                for g, group in enumerate(GROUPS):
                    if t >= GATHER_RING:
                        pool.wait_ge(turned, (t - GATHER_RING) * NG + g + 1)
                    for n in group:
                        f = GATHERED[n]
                        index = bass.IndirectOffsetOnAxis(ap=ids_sb[:, t, f:f + 1].bitcast(U32), axis=0)
                        nc.gpsimd.indirect_dma_start(rows[:, t % GATHER_RING, n, :], None, tables[f][:, :],
                                                     index).then_inc(rows_in[t][g], 16)

        def move_turned(engine, wait_ge, copy, t, g):
            wait_ge(turned, t * NG + g + 1)
            n0, n1 = FIRST_GATHERED + GROUPS[g][0], FIRST_GATHERED + GROUPS[g][-1] + 1
            bank = turn_ps[(1 + t * NG + g) % 2]
            copy(cols[:, t * P:(t + 1) * P, n0:n1].rearrange("d b n -> d n b"),
                 bank[:, 0:n1 - n0, :]).then_inc(turned_moved[engine], 1)

        def move_dots(engine, wait_ge, copy, t, quads):
            wait_ge(dots_done, t + 1)
            if t >= 2:
                wait_ge(layer1_done, 2 * (t - 1))
            if t == 0:
                wait_ge(cleared, 2)
            for s in quads:
                for q in range(2):
                    last = copy(z[QUAD * q:QUAD * (q + 1), t % 2, 0, QUAD * s:QUAD * (s + 1)],
                                dots_ps[QUAD * s:QUAD * (s + 1), :, q])
            last.then_inc(spare_moved[engine], 1)
            wait_ge(spare_moved[engine], t + 1)
            for s in quads:
                for q in range(QUADS):
                    src = dots_ps[QUAD * s:QUAD * s + NODES, :, LOW - 1 + q:NODES - 1:QUADS]
                    last = copy(z[QUAD * q:QUAD * q + NODES, t % 2, :, QUAD * s:QUAD * (s + 1)],
                                src.rearrange("i b c -> i c b"))
            last.then_inc(z_ready[engine], 1)

        @block.scalar
        def _(act):
            act.dma_start(ids_row[:], ids_picked.rearrange("(o k) b -> o k b", o=1).to_broadcast(
                [PICK_PARTS, NUM_PICKED, BATCH])).then_inc(ids_row_in, 16)
            act.dma_start(w1_sb[:], w1).then_inc(w1_in, 16)
            act.dma_start(w2_sb[:], w2.rearrange("(k p) o -> p k o", p=P)).then_inc(w2_in, 16)
            act.dma_start(w3_sb[:], w3).then_inc(small_in, 16)
            act.dma_start(b1_sb[:], b1).then_inc(small_in, 16)
            act.dma_start(b2_sb[:], b2).then_inc(small_in, 16)

            def copy(dst, src):
                return nc.scalar.activation(dst, src, ACT.Copy)

            def split_hi(k):
                act.wait_ge(table_in[k % 2], 16 * (k // 2 + 1))
                if k >= 2:
                    act.wait_ge(picked_done, k - 1)
                copy(table_hi[:, k % 2], table_raw[:, k % 2]).then_inc(hi_ready, 1)

            def move_picked(k):
                act.wait_ge(picked_done, k + 1)
                src = acc_ps[k % 2][:]
                if k == 0:
                    copy(cols[:, :, NODES + 1], src).then_inc(picked_moved, 1)
                copy(cols[:, :, 1 + k], src).then_inc(picked_moved, 1)

            split_hi(0)
            act.wait_ge(dense_turned, 1)
            copy(dense_t[:], turn_ps[0][:]).then_inc(dense_t_ready, 1)
            split_hi(1)
            for k in range(NUM_PICKED):
                move_picked(k)
                if k + 2 < NUM_PICKED:
                    split_hi(k + 2)
                if k >= NUM_PICKED - NG:
                    move_turned("scalar", act.wait_ge, copy, 0, k - (NUM_PICKED - NG))

            act.wait_ge(small_in, 48)
            for t in range(TILES):
                move_dots("scalar", act.wait_ge, copy, t, (0, 1))

                def move_groups(groups):
                    for g in groups:
                        if t + 1 < TILES and mover(t + 1, g) == "scalar":
                            move_turned("scalar", act.wait_ge, copy, t + 1, g)

                move_groups((0, 1))
                act.wait_ge(layer1_done, 2 * t + 1)
                if t >= 2:
                    act.wait_ge(layer2_done, 2 * (t - 1))
                for o in (0, 1):
                    last = nc.scalar.activation(h1[:, t % 2, o, :], acc_ps[0][:, o * P:(o + 1) * P], ACT.Relu,
                                                bias=b1_sb[:, o:o + 1])
                last.then_inc(h1_ready["scalar"], 1)
                move_groups((2, 3))
                act.wait_ge(layer2_done, 2 * t + 1)
                if t >= 2:
                    act.wait_ge(layer3_done, t - 1)
                nc.scalar.activation(h2[:, t % 2, 0, :], h2_ps[0][:, 0:P], ACT.Relu,
                                     bias=b2_sb[:, 0:1]).then_inc(h2_ready["scalar"], 1)
                move_groups((4,))

        @block.vector
        def _(dve):
            copy = nc.vector.tensor_copy
            nc.vector.memset(cols[:, :, NODES + 2:SLOTS], 0.0).then_inc(cleared, 1)
            nc.vector.memset(z[:], 0.0).then_inc(cleared, 1)

            def make_onehot(k):
                if k >= 2:
                    dve.wait_ge(picked_done, k - 1)
                for c in range(PICK_ROWS):
                    nc.vector.tensor_scalar(onehot[:, k % 2, c, :], ids_row[:, k, :],
                                            row_number[0:PICK_PARTS, c:c + 1], None,
                                            ALU.is_equal).then_inc(onehot_ready, 1)

            def split_lo(k):
                dve.wait_ge(hi_ready, k + 1)
                nc.vector.tensor_tensor(table_lo[:, k % 2], table_raw[:, k % 2], table_hi[:, k % 2],
                                        ALU.subtract).then_inc(lo_ready, 1)

            dve.wait_ge(numbers_ready, 1)
            dve.wait_ge(ids_row_in, 16)
            for k in range(NUM_PICKED):
                make_onehot(k)
                split_lo(k)
                if k == 0:
                    dve.wait_ge(dense_t_ready, 1)
                    copy(cols[:, :, 0], dense_t[:]).then_inc(dense_cols_ready, 1)
                    copy(cols[:, :, NODES], dense_t[:]).then_inc(dense_cols_ready, 1)
            dve.wait_ge(w1_in, 16)
            nc.vector.tensor_tensor(w1_sb[:, CHUNKS], w1_sb[:, CHUNKS], w1_sb[:, CHUNKS + 1],
                                    ALU.add).then_inc(w1_folded, 1)
            dve.wait_ge(small_in, 48)
            for t in range(TILES):
                move_dots("vector", dve.wait_ge, copy, t, (2, 3))

                def move_groups(groups):
                    for g in groups:
                        if t + 1 < TILES and mover(t + 1, g) == "vector":
                            move_turned("vector", dve.wait_ge, copy, t + 1, g)

                move_groups((0, 1))
                dve.wait_ge(layer1_done, 2 * t + 2)
                if t >= 2:
                    dve.wait_ge(layer2_done, 2 * (t - 1))
                for o in (2, 3):
                    last = nc.vector.tensor_scalar(h1[:, t % 2, o, :], acc_ps[1][:, (o - 2) * P:(o - 1) * P],
                                                   b1_sb[:, o:o + 1], 0.0, ALU.add, ALU.max)
                last.then_inc(h1_ready["vector"], 1)
                move_groups((2, 3))
                dve.wait_ge(layer2_done, 2 * t + 2)
                if t >= 2:
                    dve.wait_ge(layer3_done, t - 1)
                nc.vector.tensor_scalar(h2[:, t % 2, 1, :], h2_ps[1][:, 0:P], b2_sb[:, 1:2], 0.0,
                                        ALU.add, ALU.max).then_inc(h2_ready["vector"], 1)
                move_groups((4,))
                dve.wait_ge(layer3_done, t + 1)
                copy(y_sb[:, t * P:(t + 1) * P], y_ps).then_inc(y_moved, 1)

        @block.tensor
        def _(pe):
            def pick(k):
                pe.wait_ge(hi_ready, k + 1)
                if k >= 2:
                    pe.wait_ge(picked_moved, k)
                for c in range(PICK_ROWS):
                    pe.wait_ge(onehot_ready, k * PICK_ROWS + c + 1)
                    nc.tensor.matmul(acc_ps[k % 2][:], table_hi[:, k % 2, c, :], onehot[:, k % 2, c, :],
                                     start=(c == 0), stop=False)
                pe.wait_ge(lo_ready, k + 1)
                for c in range(PICK_ROWS):
                    last = nc.tensor.matmul(acc_ps[k % 2][:], table_lo[:, k % 2, c, :], onehot[:, k % 2, c, :],
                                            start=False, stop=(c == PICK_ROWS - 1))
                last.then_inc(picked_done, 1)

            def turn(t, g):
                m = t * NG + g
                pe.wait_ge(rows_in[t][g], 16 * len(GROUPS[g]))
                if m == 1:
                    pe.wait_ge(dense_t_ready, 1)
                if m >= 2:
                    before = ((m - 2) // NG, (m - 2) % NG)
                    engine = mover(*before)
                    pe.wait_ge(turned_moved[engine], moved_count(engine, *before))
                for i, n in enumerate(GROUPS[g]):
                    last = nc.tensor.transpose(turn_ps[(1 + m) % 2][:, i, :], rows[:, t % GATHER_RING, n, :],
                                               identity[:])
                last.then_inc(turned, 1)

            def dots(t):
                if t == 0:
                    pe.wait_ge(cleared, 1)
                    pe.wait_ge(dense_cols_ready, 2)
                    pe.wait_ge(picked_moved, NUM_PICKED + 1)
                for engine in ("scalar", "vector"):
                    n = moved_count(engine, t, NG - 1)
                    if n:
                        pe.wait_ge(turned_moved[engine], n)
                    if t >= 1:
                        pe.wait_ge(z_ready[engine], t)
                for b in range(QUAD):
                    for s in range(QUADS):
                        sample = t * P + QUAD * s + b
                        last = nc.tensor.matmul(dots_ps[QUAD * s:QUAD * (s + 1), b, 0:NODES - 1],
                                                cols[:, sample, :], cols[:, sample, 1:NODES],
                                                start=True, stop=True)
                last.then_inc(dots_done, 1)

            def layer1(t):
                if t == 0:
                    pe.wait_ge(w1_folded, 1)
                    pe.wait_ge(picked_moved, NUM_PICKED + 1)
                for o in range(K1):
                    if o % 2 == 0 and t >= 1:
                        pe.wait_ge(h1_ready["scalar" if o == 0 else "vector"], t)
                    psum_out = acc_ps[o // 2][:, (o % 2) * P:(o % 2 + 1) * P]
                    nc.tensor.matmul(psum_out, w1_sb[:, CHUNKS, o * P:(o + 1) * P],
                                     dense_t[:, t * P:(t + 1) * P], start=True, stop=False)
                    if o == 0:
                        pe.wait_ge(z_ready["scalar"], t + 1)
                        pe.wait_ge(z_ready["vector"], t + 1)
                    for c in range(CHUNKS):
                        last = nc.tensor.matmul(psum_out, w1_sb[:, c, o * P:(o + 1) * P], z[:, t % 2, c, :],
                                                start=False, stop=(c == CHUNKS - 1))
                    if o % 2 == 1:
                        last.then_inc(layer1_done, 1)

            def layer2(t):
                if t == 0:
                    pe.wait_ge(w2_in, 16)
                pe.wait_ge(h1_ready["scalar"], t + 1)
                for o in range(K2):
                    if o == 0 and t >= 1:
                        pe.wait_ge(h2_ready["scalar"], t)
                    if o == 1 and t >= 1:
                        pe.wait_ge(y_moved, t)
                    for k in range(K1):
                        if o == 0 and k == 2:
                            pe.wait_ge(h1_ready["vector"], t + 1)
                        last = nc.tensor.matmul(h2_ps[o][:, 0:P], w2_sb[:, k, o * P:(o + 1) * P],
                                                h1[:, t % 2, k, :], start=(k == 0), stop=(k == K1 - 1))
                    last.then_inc(layer2_done, 1)

            def layer3(t):
                if t == 0:
                    pe.wait_ge(small_in, 48)
                pe.wait_ge(h2_ready["scalar"], t + 1)
                pe.wait_ge(h2_ready["vector"], t + 1)
                for k in range(K2):
                    last = nc.tensor.matmul(y_ps, w3_sb[:, k:k + 1], h2[:, t % 2, k, :],
                                            start=(k == 0), stop=(k == K2 - 1))
                last.then_inc(layer3_done, 1)

            pe.wait_ge(identity_ready, 1)
            pe.wait_ge(dense_in, 16)
            for t in range(TILES):
                last = nc.tensor.transpose(turn_ps[0][:, t, :], dense_sb[:, t, :], identity[:])
            last.then_inc(dense_turned, 1)
            for k in range(NUM_PICKED):
                pick(k)
                if k >= NUM_PICKED - NG:
                    turn(0, k - (NUM_PICKED - NG))
            for t in range(TILES):
                def turn_next(groups):
                    for g in groups:
                        if t + 1 < TILES:
                            turn(t + 1, g)

                dots(t)
                turn_next((0, 1))
                layer1(t)
                turn_next((2, 3))
                layer2(t)
                turn_next((4,))
                layer3(t)


def kernel(**inputs):
    import concourse.bacc as bacc
    from concourse.bass_utils import run_bass_kernel_spmd

    nc = bacc.Bacc("TRN2", target_bir_lowering=False, num_devices=1)
    arrays = {}

    def declare(name, a):
        a = np.ascontiguousarray(a)
        arrays[name] = a
        return nc.dram_tensor(name, a.shape, mybir.dt.from_np(a.dtype), kind="ExternalInput").ap()

    w = np.asarray(inputs["W_top1"])
    w1 = np.zeros((P, CHUNKS + 2, H1), w.dtype)
    part, chunk, row = np.array(pair_rows()).T
    w1[part, chunk] = w[row]
    w1[:, CHUNKS] = w[:DIM]
    w1[:, CHUNKS + 1] = w[-DIM:]

    ids = np.asarray(inputs["ids"])
    out = nc.dram_tensor("out_y", (BATCH, 1), F32, kind="ExternalOutput").ap()
    build(nc,
          declare("dense", inputs["r_dense_features"]),
          declare("ids", ids),
          declare("ids_picked", ids[:, PICKED].T),
          [declare(f"tbl_{f}", inputs[f"tbl_{f}"]) for f in range(NUM_TABLES)],
          declare("w1", w1),
          declare("w2", inputs["W_top2"]),
          declare("w3", np.asarray(inputs["W_top3"]).reshape(K2, P).T),
          declare("b1", np.asarray(inputs["b_top1"]).reshape(K1, P).T),
          declare("b2", np.asarray(inputs["b_top2"]).reshape(K2, P).T),
          out)
    result = run_bass_kernel_spmd(nc, [arrays], core_ids=[0])
    return result.results[0]["out_y"]
```

```python
from contextlib import ExitStack

import concourse.bass as bass
import numpy as np
from concourse import mybir

F32 = mybir.dt.float32
F32R = mybir.dt.float32r
I32 = mybir.dt.int32
U32 = mybir.dt.uint32
ALU = mybir.AluOpType
ACT = mybir.ActivationFunctionType

P = 128
BATCH = 512
TILES = BATCH // P
DIM = 128
NUM_TABLES = 26
NODES = NUM_TABLES + 1
SLOTS = 32
QUAD = 32
QUADS = P // QUAD
TABLE_ROWS = [125000, 1250, 1000, 12500, 1000, 12500, 1250, 1000, 1250, 1000, 1000, 12500, 1000,
              1000, 12500, 1000, 1250, 12500, 1250, 12500, 1250, 1000, 1000, 1000, 1250, 1000]
PICK_PARTS = 125
PICK_ROWS = 8
ACT_CHUNKS = 1
NUM_PICKED = 8
PICKED = [f for f, rows in enumerate(TABLE_ROWS) if rows == PICK_PARTS * PICK_ROWS][:NUM_PICKED]
GATHERED = [f for f in range(NUM_TABLES) if f not in PICKED]
NODE_AT = [0] + [1 + f for f in PICKED + GATHERED]
FIRST_GATHERED = 1 + NUM_PICKED

GROUPS = [range(s, min(s + 4, len(GATHERED))) for s in range(0, len(GATHERED), 4)]
NG = len(GROUPS)
GATHER_RING = 3

LOW = 6
HIGH = NODES - 1
CHUNKS = (HIGH - LOW) // QUADS
MAIN_ROWS = HIGH - 1
REPEATS = SLOTS - NODES
SPARE_COLUMNS = {0: [HIGH], 1: list(range(1, LOW))}
H1, H2 = 512, 256
K1, K2 = H1 // P, H2 // P
FIRST_GROUPS = 2
EARLY_GROUPS = 2
H1_ACT = 3


def pair_rows():
    places = [(QUAD * ((c - LOW) % QUADS) + i, (c - LOW) // QUADS, i, c)
              for c in range(LOW, HIGH) for i in range(c)]
    for q, columns in SPARE_COLUMNS.items():
        places += [(QUAD * q + NODES + i, chunk, i, c)
                   for chunk, c in enumerate(columns) for i in range(min(c, REPEATS))]
    places += [(i, 0, i, HIGH) for i in range(LOW, HIGH)]
    places.append((QUAD + HIGH, SPARE_COLUMNS[1].index(5), 5, HIGH))
    assert len({(part, chunk) for part, chunk, _, _ in places}) == len(places)
    assert len({(i, c) for _, _, i, c in places}) == len(places) == NODES * (NODES - 1) // 2
    out = []
    for part, chunk, i, c in places:
        a, b = sorted((NODE_AT[i], NODE_AT[c]))
        out.append((part, chunk, DIM + a * NODES - a * (a + 1) // 2 + (b - a - 1)))
    return out


def mover(tile, group):
    return "scalar" if tile == 0 or group % 2 == 0 else "vector"


def early_groups(t):
    return EARLY_GROUPS + (FIRST_GROUPS if t == 0 else 0)


def moved_count(engine, tile, group):
    return sum(mover(t, g) == engine for t in range(tile + 1) for g in range(NG)
               if (t, g) <= (tile, group))


def build(nc, dense, ids, ids_picked, tables, w1, w2, w3, b1, b2, out):
    with ExitStack() as ctx:
        def sb(name, shape, dt=F32):
            return ctx.enter_context(nc.sbuf_tensor(name, shape, dt))

        def psum(name, shape):
            return ctx.enter_context(nc.psum_tensor(name, shape, F32))

        def sem(name):
            return ctx.enter_context(nc.semaphore(name))

        ids_sb = sb("ids_sb", [P, TILES, NUM_TABLES], I32)
        ids_row = sb("ids_row", [PICK_PARTS, NUM_PICKED, BATCH], I32)
        dense_sb = sb("dense_sb", [P, TILES, DIM])
        w1_sb = sb("w1_sb", [P, CHUNKS + 2, H1])
        w2_sb = sb("w2_sb", [P, K1, H2])
        w3_sb = sb("w3_sb", [P, K2])
        b1_sb = sb("b1_sb", [P, K1])
        b2_sb = sb("b2_sb", [P, K2])
        identity = sb("identity", [P, P])
        row_number = sb("row_number", [P, PICK_ROWS])
        minus_row = sb("minus_row", [P, PICK_ROWS])
        distance = sb("distance", [PICK_PARTS, ACT_CHUNKS, BATCH])
        table_raw = sb("table_raw", [PICK_PARTS, 2, PICK_ROWS, DIM])
        table_hi = sb("table_hi", [PICK_PARTS, 2, PICK_ROWS, DIM], F32R)
        table_lo = sb("table_lo", [PICK_PARTS, 2, PICK_ROWS, DIM], F32R)
        onehot = sb("onehot", [PICK_PARTS, 2, PICK_ROWS, BATCH], F32R)
        rows = sb("rows", [P, GATHER_RING, len(GATHERED), DIM])
        dense_t = sb("dense_t", [DIM, BATCH])
        cols = sb("cols", [DIM, BATCH, SLOTS])
        z = sb("z", [P, 2, CHUNKS, P])
        h1 = sb("h1", [P, 2, K1, P])
        h2 = sb("h2", [P, 2, K2, P])
        y_sb = sb("y_sb", [1, BATCH])

        acc_ps = [psum("acc_ps0", [P, 512]), psum("acc_ps1", [P, 512])]
        turn_ps = [psum("turn_ps0", [P, 4, P]), psum("turn_ps1", [P, 4, P])]
        dots_ps = psum("dots_ps", [P, QUAD, SLOTS])
        h2_ps = [psum("h2_ps0", [P, 512]), psum("h2_ps1", [P, 512])]
        y_ps = h2_ps[1][0:1, P:2 * P]

        ids_in = sem("ids_in")
        ids_row_in = [sem(f"ids_row_in{i}") for i in range(3)]
        dense_in = sem("dense_in")
        w1_in = sem("w1_in")
        w2_in = sem("w2_in")
        small_in = sem("small_in")
        table_in = [sem("table_in0"), sem("table_in1")]
        rows_in = [[sem(f"rows_in{t}_{g}") for g in range(NG)] for t in range(TILES)]
        ones_ready = sem("ones_ready")
        identity_ready = sem("identity_ready")
        numbers_ready = sem("numbers_ready")
        cleared = sem("cleared")
        hi_ready = sem("hi_ready")
        lo_ready = sem("lo_ready")
        onehot_ready = {"scalar": sem("onehot_ready_act"), "vector": sem("onehot_ready_dve")}
        distance_ready = sem("distance_ready")
        picked_done = sem("picked_done")
        picked_moved = sem("picked_moved")
        dense_turned = sem("dense_turned")
        dense_moved = sem("dense_moved")
        turned = sem("turned")
        turned_moved = {"scalar": sem("turned_moved_act"), "vector": sem("turned_moved_dve")}
        dots_done = sem("dots_done")
        spare_moved = {"scalar": sem("spare_moved_act"), "vector": sem("spare_moved_dve")}
        z_ready = {"scalar": sem("z_ready_act"), "vector": sem("z_ready_dve")}
        w1_folded = sem("w1_folded")
        layer1_done = sem("layer1_done")
        h1_ready = {"scalar": sem("h1_ready_act"), "vector": sem("h1_ready_dve")}
        layer2_done = sem("layer2_done")
        h2_ready = {"scalar": sem("h2_ready_act"), "vector": sem("h2_ready_dve")}
        layer3_done = sem("layer3_done")
        y_moved = sem("y_moved")
        out_done = sem("out_done")

        block = ctx.enter_context(nc.Block())

        @block.sync
        def _(sp):
            def load_ids_row(k0, k1, loaded):
                src = ids_picked[k0:k1].rearrange("(o k) b -> o k b", o=1)
                sp.dma_start(ids_row[:, k0:k1], src.to_broadcast([PICK_PARTS, k1 - k0, BATCH])).then_inc(loaded, 16)


            def load_table(k):
                src = tables[PICKED[k]].rearrange("(p c) d -> p c d", c=PICK_ROWS)
                sp.dma_start(table_raw[:, k % 2], src).then_inc(table_in[k % 2], 16)

            load_ids_row(0, 1, ids_row_in[0])
            load_table(0)
            sp.dma_start(dense_sb[:], dense.rearrange("(t p) d -> p t d", p=P)).then_inc(dense_in, 16)
            load_ids_row(1, 2, ids_row_in[1])
            load_table(1)
            load_ids_row(2, NUM_PICKED, ids_row_in[2])
            for k in range(2, NUM_PICKED):
                sp.wait_ge(lo_ready, k - 1)
                load_table(k)
            sp.dma_start(w1_sb[:], w1).then_inc(w1_in, 16)
            sp.dma_start(w2_sb[:], w2.rearrange("(k p) o -> p k o", p=P)).then_inc(w2_in, 16)
            sp.dma_start(w3_sb[:], w3).then_inc(small_in, 16)
            sp.dma_start(b1_sb[:], b1).then_inc(small_in, 16)
            sp.dma_start(b2_sb[:], b2).then_inc(small_in, 16)
            sp.wait_ge(y_moved, TILES)
            sp.dma_start(out.rearrange("(o b) c -> o (b c)", o=1), y_sb[:]).then_inc(out_done, 16)
            sp.wait_ge(out_done, 16)

        @block.gpsimd
        def _(pool):
            nc.gpsimd.iota(row_number[:], pattern=[[1, PICK_ROWS]], base=0, channel_multiplier=PICK_ROWS,
                           allow_small_or_imprecise_dtypes=True).then_inc(numbers_ready, 1)
            nc.gpsimd.iota(minus_row[:], pattern=[[-1, PICK_ROWS]], base=0, channel_multiplier=-PICK_ROWS,
                           allow_small_or_imprecise_dtypes=True).then_inc(numbers_ready, 1)
            nc.gpsimd.memset(identity[:], 1.0).then_inc(ones_ready, 1)
            pool.wait_ge(ones_ready, 1)
            nc.gpsimd.affine_select(out=identity[:], in_=identity[:], compare_op=ALU.is_equal, fill=0.0,
                                    base=0, pattern=[[-1, P]],
                                    channel_multiplier=1).then_inc(identity_ready, 1)
            pool.wait_ge(ids_in, 16)
            for t in range(TILES):
                for g, group in enumerate(GROUPS):
                    if t >= GATHER_RING:
                        pool.wait_ge(turned, (t - GATHER_RING) * NG + g + 1)
                    for n in group:
                        f = GATHERED[n]
                        index = bass.IndirectOffsetOnAxis(ap=ids_sb[:, t, f:f + 1].bitcast(U32), axis=0)
                        nc.gpsimd.indirect_dma_start(rows[:, t % GATHER_RING, n, :], None, tables[f][:, :],
                                                     index).then_inc(rows_in[t][g], 16)

        def move_turned(engine, wait_ge, copy, t, g):
            wait_ge(turned, t * NG + g + 1)
            n0, n1 = FIRST_GATHERED + GROUPS[g][0], FIRST_GATHERED + GROUPS[g][-1] + 1
            bank = turn_ps[(1 + t * NG + g) % 2]
            copy(cols[:, t * P:(t + 1) * P, n0:n1].rearrange("d b n -> d n b"),
                 bank[:, 0:n1 - n0, :]).then_inc(turned_moved[engine], 1)

        def move_dots(engine, wait_ge, copy, t, s, half):
            wait_ge(dots_done, 2 * t + half + 1)
            if t >= 2:
                wait_ge(layer1_done, 2 * (t - 1))
            if t == 0:
                wait_ge(cleared, 1)
            samples = slice(QUAD * s, QUAD * (s + 1))
            for q, columns in SPARE_COLUMNS.items():
                c0, n = columns[0] - 1, len(columns)
                last = copy(z[QUAD * q:QUAD * (q + 1), t % 2, 0:n, samples],
                            dots_ps[samples, :, c0:c0 + n].rearrange("i b c -> i c b"))
            last.then_inc(spare_moved[engine], 1)

            def move_main(q):
                first = 1 if q == 0 else 0
                src = dots_ps[QUAD * s:QUAD * s + MAIN_ROWS, :, LOW - 1 + q + QUADS * first:HIGH - 1:QUADS]
                return copy(z[QUAD * q:QUAD * q + MAIN_ROWS, t % 2, first:CHUNKS, samples],
                            src.rearrange("i b c -> i c b"))

            for q in range(len(SPARE_COLUMNS), QUADS):
                move_main(q)
            copied = 2 * t + half + 1
            wait_ge(spare_moved[engine], copied)
            copy(z[0:LOW, t % 2, 0, samples], dots_ps[QUAD * s:QUAD * s + LOW, :, LOW - 1])
            for q in SPARE_COLUMNS:
                last = move_main(q)
            last.then_inc(z_ready[engine], 1)

        @block.scalar
        def _(act):
            act.dma_start(ids_sb[:], ids.rearrange("(t p) f -> p t f", p=P)).then_inc(ids_in, 16)

            def copy(dst, src):
                return nc.scalar.activation(dst, src, ACT.Copy)

            def split_hi(k):
                act.wait_ge(table_in[k % 2], 16 * (k // 2 + 1))
                if k >= 2:
                    act.wait_ge(picked_done, k - 1)
                copy(table_hi[:, k % 2], table_raw[:, k % 2]).then_inc(hi_ready, 1)

            def make_onehot(k):
                if k < 3:
                    act.wait_ge(ids_row_in[k], 16)
                if k == 0:
                    act.wait_ge(numbers_ready, 2)
                if k >= 1:
                    act.wait_ge(onehot_ready["scalar"], ACT_CHUNKS * k)
                for i in range(ACT_CHUNKS):
                    c = PICK_ROWS - ACT_CHUNKS + i
                    nc.scalar.activation(distance[:, i, :], ids_row[:, k, :], ACT.Abs,
                                         bias=minus_row[0:PICK_PARTS, c:c + 1]).then_inc(distance_ready, 1)
                for i in range(ACT_CHUNKS):
                    act.wait_ge(distance_ready, ACT_CHUNKS * k + i + 1)
                    nc.scalar.activation(onehot[:, k % 2, PICK_ROWS - ACT_CHUNKS + i, :], distance[:, i, :],
                                         ACT.Relu, bias=1.0, scale=-1.0).then_inc(onehot_ready["scalar"], 1)

            def move_picked(k):
                act.wait_ge(picked_done, k + 1)
                src = acc_ps[k % 2][:]
                if 1 + k < REPEATS:
                    copy(cols[:, :, NODES + 1 + k], src)
                copy(cols[:, :, 1 + k], src).then_inc(picked_moved, 1)

            split_hi(0)
            make_onehot(0)
            act.wait_ge(dense_turned, 1)
            dense_turned_ps = turn_ps[0][:].rearrange("d t b -> d (t b)")
            copy(dense_t[:], dense_turned_ps)
            copy(cols[:, :, 0], dense_turned_ps)
            copy(cols[:, :, NODES], dense_turned_ps).then_inc(dense_moved, 1)
            split_hi(1)
            make_onehot(1)
            for k in range(NUM_PICKED):
                if k >= NUM_PICKED - NG:
                    move_turned("scalar", act.wait_ge, copy, 0, k - (NUM_PICKED - NG))
                move_picked(k)
                if k + 2 < NUM_PICKED:
                    split_hi(k + 2)
                    make_onehot(k + 2)

            act.wait_ge(small_in, 48)

            def activate2(t):
                act.wait_ge(layer2_done, 2 * t + 1)
                if t >= 2:
                    act.wait_ge(layer3_done, t - 1)
                nc.scalar.activation(h2[:, t % 2, 0, :], h2_ps[0][:, 0:P], ACT.Relu,
                                     bias=b2_sb[:, 0:1]).then_inc(h2_ready["scalar"], 1)

            def move_groups(t, groups):
                for g in groups:
                    if t < TILES and mover(t, g) == "scalar":
                        move_turned("scalar", act.wait_ge, copy, t, g)

            move_groups(1, range(FIRST_GROUPS))
            for t in range(TILES):
                for half in range(2):
                    move_dots("scalar", act.wait_ge, copy, t, 2 * half, half)
                move_groups(t + 1, range(FIRST_GROUPS if t == 0 else 0, early_groups(t)))
                act.wait_ge(layer1_done, 2 * t + 1)
                if t >= 2:
                    act.wait_ge(layer2_done, 2 * (t - 1))
                for o in range(H1_ACT):
                    last = nc.scalar.activation(h1[:, t % 2, o, :], acc_ps[0][:, o * P:(o + 1) * P], ACT.Relu,
                                                bias=b1_sb[:, o:o + 1])
                last.then_inc(h1_ready["scalar"], 1)
                move_groups(t + 1, range(early_groups(t), NG))
                activate2(t)

        @block.vector
        def _(dve):
            copy = nc.vector.tensor_copy
            nc.vector.memset(z[:], 0.0).then_inc(cleared, 1)

            def make_onehot(k):
                if k >= 2:
                    dve.wait_ge(picked_done, k - 1)
                for c in range(PICK_ROWS - ACT_CHUNKS):
                    nc.vector.tensor_scalar(onehot[:, k % 2, c, :], ids_row[:, k, :],
                                            row_number[0:PICK_PARTS, c:c + 1], None,
                                            ALU.is_equal).then_inc(onehot_ready["vector"], 1)

            def split_lo(k):
                dve.wait_ge(hi_ready, k + 1)
                nc.vector.tensor_tensor(table_lo[:, k % 2], table_raw[:, k % 2], table_hi[:, k % 2],
                                        ALU.subtract).then_inc(lo_ready, 1)

            dve.wait_ge(numbers_ready, 1)
            for k in range(NUM_PICKED):
                if k < 3:
                    dve.wait_ge(ids_row_in[k], 16)
                make_onehot(k)
                split_lo(k)
            dve.wait_ge(w1_in, 16)
            nc.vector.tensor_tensor(w1_sb[:, CHUNKS], w1_sb[:, CHUNKS], w1_sb[:, CHUNKS + 1],
                                    ALU.add).then_inc(w1_folded, 1)
            dve.wait_ge(small_in, 48)

            def activate2(t):
                dve.wait_ge(layer2_done, 2 * t + 2)
                if t >= 2:
                    dve.wait_ge(layer3_done, t - 1)
                nc.vector.tensor_scalar(h2[:, t % 2, 1, :], h2_ps[1][:, 0:P], b2_sb[:, 1:2], 0.0,
                                        ALU.add, ALU.max).then_inc(h2_ready["vector"], 1)

            def move_groups(t, groups):
                for g in groups:
                    if t < TILES and mover(t, g) == "vector":
                        move_turned("vector", dve.wait_ge, copy, t, g)

            def move_y(t):
                dve.wait_ge(layer3_done, t + 1)
                copy(y_sb[:, t * P:(t + 1) * P], y_ps).then_inc(y_moved, 1)

            move_groups(1, range(FIRST_GROUPS))
            for t in range(TILES):
                for half in range(2):
                    move_dots("vector", dve.wait_ge, copy, t, 2 * half + 1, half)
                if t >= 1:
                    move_y(t - 1)
                move_groups(t + 1, range(FIRST_GROUPS if t == 0 else 0, early_groups(t)))
                dve.wait_ge(layer1_done, 2 * t + 2)
                if t >= 2:
                    dve.wait_ge(layer2_done, 2 * (t - 1))
                for o in range(H1_ACT, K1):
                    last = nc.vector.tensor_scalar(h1[:, t % 2, o, :], acc_ps[1][:, o * P:(o + 1) * P],
                                                   b1_sb[:, o:o + 1], 0.0, ALU.add, ALU.max)
                last.then_inc(h1_ready["vector"], 1)
                move_groups(t + 1, range(early_groups(t), NG))
                activate2(t)
            move_y(TILES - 1)

        @block.tensor
        def _(pe):
            def pick(k):
                pe.wait_ge(hi_ready, k + 1)
                if k >= 2:
                    pe.wait_ge(picked_moved, k - 1)
                for c in range(PICK_ROWS):
                    by_dve = PICK_ROWS - ACT_CHUNKS
                    if c < by_dve:
                        pe.wait_ge(onehot_ready["vector"], k * by_dve + c + 1)
                    else:
                        pe.wait_ge(onehot_ready["scalar"], k * ACT_CHUNKS + c - by_dve + 1)
                    nc.tensor.matmul(acc_ps[k % 2][:], table_hi[:, k % 2, c, :], onehot[:, k % 2, c, :],
                                     start=(c == 0), stop=False)
                if k >= NUM_PICKED - NG:
                    turn(0, k - (NUM_PICKED - NG))
                pe.wait_ge(lo_ready, k + 1)
                for c in range(PICK_ROWS):
                    last = nc.tensor.matmul(acc_ps[k % 2][:], table_lo[:, k % 2, c, :], onehot[:, k % 2, c, :],
                                            start=False, stop=(c == PICK_ROWS - 1))
                last.then_inc(picked_done, 1)

            def turn(t, g):
                m = t * NG + g
                pe.wait_ge(rows_in[t][g], 16 * len(GROUPS[g]))
                if m == 1:
                    pe.wait_ge(dense_moved, 1)
                if m >= 2:
                    before = ((m - 2) // NG, (m - 2) % NG)
                    engine = mover(*before)
                    pe.wait_ge(turned_moved[engine], moved_count(engine, *before))
                for i, n in enumerate(GROUPS[g]):
                    last = nc.tensor.transpose(turn_ps[(1 + m) % 2][:, i, :], rows[:, t % GATHER_RING, n, :],
                                               identity[:])
                last.then_inc(turned, 1)

            def dots(t, between):
                if t == 0:
                    pe.wait_ge(dense_moved, 1)
                    pe.wait_ge(picked_moved, NUM_PICKED)
                for engine in ("scalar", "vector"):
                    n = moved_count(engine, t, NG - 1)
                    if n:
                        pe.wait_ge(turned_moved[engine], n)
                    if t >= 1:
                        pe.wait_ge(z_ready[engine], 2 * t)
                for half in range(2):
                    for b in range(QUAD):
                        for s in (2 * half, 2 * half + 1):
                            sample = t * P + QUAD * s + b
                            last = nc.tensor.matmul(dots_ps[QUAD * s:QUAD * (s + 1), b, 0:NODES - 1],
                                                    cols[:, sample, :], cols[:, sample, 1:NODES],
                                                    start=True, stop=True)
                    last.then_inc(dots_done, 1)
                    if half == 0:
                        between()

            def layer1(t):
                if t == 0:
                    pe.wait_ge(w1_folded, 1)
                    pe.wait_ge(picked_moved, NUM_PICKED)
                def block(o):
                    return acc_ps[0 if o < H1_ACT else 1][:, o * P:(o + 1) * P]

                for o in range(K1):
                    if t >= 1 and o in (0, H1_ACT):
                        pe.wait_ge(h1_ready["scalar" if o == 0 else "vector"], t)
                    nc.tensor.matmul(block(o), w1_sb[:, CHUNKS, o * P:(o + 1) * P],
                                     dense_t[:, t * P:(t + 1) * P], start=o in (0, H1_ACT), stop=False,
                                     skip_group_check=True)
                pe.wait_ge(z_ready["scalar"], 2 * t + 2)
                pe.wait_ge(z_ready["vector"], 2 * t + 2)
                for o in range(K1):
                    for c in range(CHUNKS):
                        last = nc.tensor.matmul(block(o), w1_sb[:, c, o * P:(o + 1) * P], z[:, t % 2, c, :],
                                                start=False, stop=(c == CHUNKS - 1), skip_group_check=True)
                    if o in (H1_ACT - 1, K1 - 1):
                        last.then_inc(layer1_done, 1)

            def layer2(t, part):
                if t == 0:
                    pe.wait_ge(w2_in, 16)
                if part == 0 and t >= 1:
                    pe.wait_ge(h2_ready["scalar"], t)
                    pe.wait_ge(y_moved, t)
                pe.wait_ge(h1_ready["vector" if part else "scalar"], t + 1)
                for o in range(K2):
                    for k in range(H1_ACT, K1) if part else range(H1_ACT):
                        last = nc.tensor.matmul(h2_ps[o][:, 0:P], w2_sb[:, k, o * P:(o + 1) * P],
                                                h1[:, t % 2, k, :], start=(k == 0), stop=(k == K1 - 1))
                    if part == 1:
                        last.then_inc(layer2_done, 1)

            def layer3(t):
                if t == 0:
                    pe.wait_ge(small_in, 48)
                pe.wait_ge(h2_ready["scalar"], t + 1)
                pe.wait_ge(h2_ready["vector"], t + 1)
                for k in range(K2):
                    last = nc.tensor.matmul(y_ps, w3_sb[:, k:k + 1], h2[:, t % 2, k, :],
                                            start=(k == 0), stop=(k == K2 - 1))
                last.then_inc(layer3_done, 1)

            pe.wait_ge(identity_ready, 1)
            pe.wait_ge(dense_in, 16)
            for t in range(TILES):
                last = nc.tensor.transpose(turn_ps[0][:, t, :], dense_sb[:, t, :], identity[:])
            last.then_inc(dense_turned, 1)
            for k in range(NUM_PICKED):
                pick(k)
            for t in range(TILES):
                more = t + 1 < TILES
                if t == 0:
                    for g in range(FIRST_GROUPS):
                        turn(1, g)
                dots(t, between=lambda: layer3(t - 1) if 1 <= t < TILES - 1 else None)
                if t == TILES - 1:
                    layer3(t - 1)
                if more:
                    for g in range(FIRST_GROUPS if t == 0 else 0, early_groups(t)):
                        turn(t + 1, g)
                layer1(t)
                if more:
                    for g in range(early_groups(t), NG - 1):
                        turn(t + 1, g)
                layer2(t, 0)
                if more:
                    turn(t + 1, NG - 1)
                layer2(t, 1)
            layer3(TILES - 1)


def kernel(**inputs):
    import concourse.bacc as bacc
    from concourse.bass_utils import run_bass_kernel_spmd

    nc = bacc.Bacc("TRN2", target_bir_lowering=False, num_devices=1)
    arrays = {}

    def declare(name, a):
        a = np.ascontiguousarray(a)
        arrays[name] = a
        return nc.dram_tensor(name, a.shape, mybir.dt.from_np(a.dtype), kind="ExternalInput").ap()

    w = np.asarray(inputs["W_top1"])
    w1 = np.zeros((P, CHUNKS + 2, H1), w.dtype)
    part, chunk, row = np.array(pair_rows()).T
    w1[part, chunk] = w[row]
    w1[:, CHUNKS] = w[:DIM]
    w1[:, CHUNKS + 1] = w[-DIM:]

    ids = np.asarray(inputs["ids"])
    out = nc.dram_tensor("out_y", (BATCH, 1), F32, kind="ExternalOutput").ap()
    build(nc,
          declare("dense", inputs["r_dense_features"]),
          declare("ids", ids),
          declare("ids_picked", ids[:, PICKED].T),
          [declare(f"tbl_{f}", inputs[f"tbl_{f}"]) for f in range(NUM_TABLES)],
          declare("w1", w1),
          declare("w2", inputs["W_top2"]),
          declare("w3", np.asarray(inputs["W_top3"]).reshape(K2, P).T),
          declare("b1", np.asarray(inputs["b_top1"]).reshape(K1, P).T),
          declare("b2", np.asarray(inputs["b_top2"]).reshape(K2, P).T),
          out)
    result = run_bass_kernel_spmd(nc, [arrays], core_ids=[0])
    return result.results[0]["out_y"]
```
